# Optimizing a Trainium2 kernel written in Bass

```python
import numpy as np
import jax
import jax.numpy as jnp

def _softmax(x, axis=-1):
    return jax.nn.softmax(x, axis=axis)

def _gelu(x):
    return jax.nn.gelu(x, approximate=True)

def _silu(x):
    return jax.nn.silu(x)

def _sigmoid(x):
    return jax.nn.sigmoid(x)

def _layernorm(x, axis=-1, eps=1e-05):
    m = jnp.mean(x, axis=axis, keepdims=True)
    v = jnp.var(x, axis=axis, keepdims=True)
    return (x - m) / jnp.sqrt(v + eps)

def _scatter_add(tgt, idx, src, axis=0):
    return tgt.at[idx].add(src)

def _segment_sum(src, seg, n):
    return jax.ops.segment_sum(src, seg, n)
kernel_name = 'mk_xattn_seq_d2_seqx_r4_b05c26'

def setup_inputs(seed: int=0):
    np.random.seed(seed)
    _w = jnp.asarray

    def _rec_inputs():
        import jax
        import jax.numpy as jnp
        _rk = jax.random.key(seed)
        x = -0.0005207 + 1.001 * jax.random.normal(jax.random.fold_in(_rk, 1), (16, 512, 256), jnp.float32)
        _lenS = 512 - jax.random.randint(jax.random.fold_in(_rk, 7), (16,), 0, max(1, 512 // 4) + 1, jnp.int32)
        _lenS2 = 1601 - jax.random.randint(jax.random.fold_in(_rk, 8), (16,), 0, max(1, 1601 // 4) + 1, jnp.int32)
        _ctx_1024P = jax.random.normal(jax.random.fold_in(_rk, 11), (16, 16, 256), jnp.float32)
        _ctx_1024c = jax.random.dirichlet(jax.random.fold_in(_rk, 511), 0.3 * jnp.ones((16,), jnp.float32), (16, 1601))
        _ctx_1024t = jnp.einsum('bsk,bkd->bsd', _ctx_1024c, _ctx_1024P)
        _ctx_1024t = _ctx_1024t * jax.lax.rsqrt(jnp.mean(jnp.square(_ctx_1024t)) + 1e-12) * 0.953939
        ctx_1024 = -1.39393e-06 + 0.999914 * (_ctx_1024t + 0.3 * jax.random.normal(jax.random.fold_in(_rk, 611), (16, 1601, 256), jnp.float32))
        _validS = jnp.arange(512)[None, :] < _lenS[:, None]
        _validS2 = jnp.arange(1601)[None, :] < _lenS2[:, None]
        _causal = jnp.tril(jnp.ones((512, 512), dtype=bool))
        mask_BxSxS2_ik1 = jnp.where(jnp.broadcast_to(_validS2[:, None, :], (16, 512, 1601)), 1, 0).astype(jnp.int32)
        mask_1xS2_bf0 = jnp.logical_not(jnp.ones((1, 1601), dtype=bool))
        return (x, ctx_1024, mask_BxSxS2_ik1, mask_1xS2_bf0)
    x, ctx_1024, mask_BxSxS2_ik1, mask_1xS2_bf0 = _rec_inputs()

    def _L0_xattn_setup():
        import jax, jax.numpy as jnp
        import numpy as np
        H = 256
        NH = 16
        HD = H // NH
        EPS = 1e-05

        def _split_heads(x, B, L):
            return x.reshape(B, L, NH, HD).transpose(0, 2, 1, 3)
        key = jax.random.key(seed)
        ks = jax.random.split(key, 16)
        B, LQ, LK = (2, 256, 512)
        s = 1.0 / np.sqrt(H)
        inp = {'query': jax.random.normal(ks[0], (B, LQ, H), jnp.float32), 'key': jax.random.normal(ks[1], (B, LK, H), jnp.float32), 'value': jax.random.normal(ks[2], (B, LK, H), jnp.float32), 'mask': jax.random.randint(ks[3], (B, LQ, LK), 0, 2, jnp.int32), 'Wq': jax.random.normal(ks[4], (H, H), jnp.float32) * s, 'bq': jnp.zeros((H,), jnp.float32), 'Wk': jax.random.normal(ks[5], (H, H), jnp.float32) * s, 'bk': jnp.zeros((H,), jnp.float32), 'Wv': jax.random.normal(ks[6], (H, H), jnp.float32) * s, 'bv': jnp.zeros((H,), jnp.float32), 'Wo': jax.random.normal(ks[7], (H, H), jnp.float32) * s, 'bo': jnp.zeros((H,), jnp.float32), 'ln_g': jnp.ones((H,), jnp.float32), 'ln_b': jnp.zeros((H,), jnp.float32)}
        return inp
    _L0_xattn_all = _L0_xattn_setup()
    _L0_xattn_in = {k: v for k, v in _L0_xattn_all.items() if k in ('Wq', 'bq', 'Wk', 'bk', 'Wv', 'bv', 'Wo', 'bo', 'ln_g', 'ln_b')}
    del _L0_xattn_all

    def _L1_xattn_setup():
        import jax, jax.numpy as jnp
        import numpy as np
        D = 256
        D_STATE = 128
        N_HEADS = 8
        D_INNER = 2 * D
        HEADDIM = 64
        H_M = D_INNER // HEADDIM
        D_CONV = 4
        CONV_DIM = D_INNER + 2 * D_STATE
        D_IN_PROJ = 2 * D_INNER + 2 * D_STATE + H_M
        B = 1
        LQ = 256
        LK = 512
        EPS = 1e-05

        def _rms(x, w):
            return x * jax.lax.rsqrt(jnp.mean(x * x, axis=-1, keepdims=True) + EPS) * w

        def _ln(x, w, b):
            mu = jnp.mean(x, axis=-1, keepdims=True)
            v = jnp.mean((x - mu) ** 2, axis=-1, keepdims=True)
            return (x - mu) * jax.lax.rsqrt(v + EPS) * w + b

        def _mamba2_block(x, norm_w, in_proj_w, conv_w, conv_b, dt_bias, A_log, D_skip, gnorm_w, out_proj_w):
            b, L, _ = x.shape
            resid = x
            zxbcdt = _rms(x, norm_w) @ in_proj_w
            z = zxbcdt[..., :D_INNER]
            xBC = zxbcdt[..., D_INNER:D_INNER + CONV_DIM]
            dt = jax.nn.softplus(zxbcdt[..., -H_M:] + dt_bias)
            padded = jnp.pad(xBC, ((0, 0), (D_CONV - 1, 0), (0, 0)))
            conv = conv_b + sum((padded[:, k:k + L, :] * conv_w[:, k] for k in range(D_CONV)))
            xBC = jax.nn.silu(conv)
            xh = xBC[..., :D_INNER].reshape(b, L, H_M, HEADDIM)
            Bm = xBC[..., D_INNER:D_INNER + D_STATE]
            Cm = xBC[..., D_INNER + D_STATE:]
            A = -jnp.exp(A_log)
            decay = jnp.exp(dt * A)
            dbx = dt[..., None] * xh

            def step(h, inp):
                dec, u, bt, ct = inp
                h = h * dec[:, :, None, None] + u[..., None] * bt[:, None, None, :]
                y = jnp.einsum('bhpn,bn->bhp', h, ct)
                return (h, y)
            h0 = jnp.zeros((b, H_M, HEADDIM, D_STATE), x.dtype)
            xs = (decay.transpose(1, 0, 2), dbx.transpose(1, 0, 2, 3), Bm.transpose(1, 0, 2), Cm.transpose(1, 0, 2))
            _, ys = jax.lax.scan(step, h0, xs)
            y = ys.transpose(1, 0, 2, 3) + D_skip[None, None, :, None] * xh
            u = _rms(y.reshape(b, L, D_INNER) * jax.nn.silu(z), gnorm_w)
            return resid + u @ out_proj_w

        def _cross_attention(x, enc, pad_mask, ln_w, ln_b, Wq, Wk, Wv, Wo):
            b, Lq, _ = x.shape
            Lk = enc.shape[1]
            dh = D // N_HEADS
            resid = x
            xn = _ln(x, ln_w, ln_b)
            q = (xn @ Wq).reshape(b, Lq, N_HEADS, dh)
            k = (enc @ Wk).reshape(b, Lk, N_HEADS, dh)
            v = (enc @ Wv).reshape(b, Lk, N_HEADS, dh)
            scores = jnp.einsum('bqhd,bkhd->bhqk', q, k) * np.float32(1.0 / np.sqrt(dh))
            scores = jnp.where(pad_mask[:, None, None, :], jnp.float32(-1000000000.0), scores)
            p = jax.nn.softmax(scores, axis=-1)
            ctx = jnp.einsum('bhqk,bkhd->bqhd', p, v).reshape(b, Lq, D)
            return resid + ctx @ Wo
        key = jax.random.key(seed)
        ks = jax.random.split(key, 10)
        s = 0.02
        return {'x': jax.random.normal(ks[0], (B, LQ, D), jnp.float32), 'encoder_out': jax.random.normal(ks[1], (B, LK, D), jnp.float32), 'encoder_padding_mask': jnp.zeros((B, LK), dtype=bool), 'm_norm_w': jnp.ones((D,), jnp.float32), 'in_proj_w': s * jax.random.normal(ks[2], (D, D_IN_PROJ), jnp.float32), 'conv_w': s * jax.random.normal(ks[3], (CONV_DIM, D_CONV), jnp.float32), 'conv_b': jnp.zeros((CONV_DIM,), jnp.float32), 'dt_bias': jnp.full((H_M,), float(np.log(np.expm1(0.01))), jnp.float32), 'A_log': jnp.log(jnp.linspace(1.0, 16.0, H_M)).astype(jnp.float32), 'D_skip': jnp.ones((H_M,), jnp.float32), 'gnorm_w': jnp.ones((D_INNER,), jnp.float32), 'out_proj_w': s * jax.random.normal(ks[4], (D_INNER, D), jnp.float32), 'ca_ln_w': jnp.ones((D,), jnp.float32), 'ca_ln_b': jnp.zeros((D,), jnp.float32), 'Wq': s * jax.random.normal(ks[5], (D, D), jnp.float32), 'Wk': s * jax.random.normal(ks[6], (D, D), jnp.float32), 'Wv': s * jax.random.normal(ks[7], (D, D), jnp.float32), 'Wo': s * jax.random.normal(ks[8], (D, D), jnp.float32)}
    _L1_xattn_all = _L1_xattn_setup()
    _L1_xattn_in = {k: v for k, v in _L1_xattn_all.items() if k in ('m_norm_w', 'in_proj_w', 'conv_w', 'conv_b', 'dt_bias', 'A_log', 'D_skip', 'gnorm_w', 'out_proj_w', 'ca_ln_w', 'ca_ln_b', 'Wq', 'Wk', 'Wv', 'Wo')}
    del _L1_xattn_all
    return {'x': x, 'ctx_1024': ctx_1024, 'mask_BxSxS2_ik1': mask_BxSxS2_ik1, 'mask_1xS2_bf0': mask_1xS2_bf0, 'L0_xattn_Wq': _L0_xattn_in['Wq'], 'L0_xattn_bq': _L0_xattn_in['bq'], 'L0_xattn_Wk': _L0_xattn_in['Wk'], 'L0_xattn_bk': _L0_xattn_in['bk'], 'L0_xattn_Wv': _L0_xattn_in['Wv'], 'L0_xattn_bv': _L0_xattn_in['bv'], 'L0_xattn_Wo': _L0_xattn_in['Wo'], 'L0_xattn_bo': _L0_xattn_in['bo'], 'L0_xattn_ln_g': _L0_xattn_in['ln_g'], 'L0_xattn_ln_b': _L0_xattn_in['ln_b'], 'L1_xattn_m_norm_w': _L1_xattn_in['m_norm_w'], 'L1_xattn_in_proj_w': _L1_xattn_in['in_proj_w'], 'L1_xattn_conv_w': _L1_xattn_in['conv_w'], 'L1_xattn_conv_b': _L1_xattn_in['conv_b'], 'L1_xattn_dt_bias': _L1_xattn_in['dt_bias'], 'L1_xattn_A_log': _L1_xattn_in['A_log'], 'L1_xattn_D_skip': _L1_xattn_in['D_skip'], 'L1_xattn_gnorm_w': _L1_xattn_in['gnorm_w'], 'L1_xattn_out_proj_w': _L1_xattn_in['out_proj_w'], 'L1_xattn_ca_ln_w': _L1_xattn_in['ca_ln_w'], 'L1_xattn_ca_ln_b': _L1_xattn_in['ca_ln_b'], 'L1_xattn_Wq': _L1_xattn_in['Wq'], 'L1_xattn_Wk': _L1_xattn_in['Wk'], 'L1_xattn_Wv': _L1_xattn_in['Wv'], 'L1_xattn_Wo': _L1_xattn_in['Wo']}

def reference(x, ctx_1024, mask_BxSxS2_ik1, mask_1xS2_bf0, L0_xattn_Wq, L0_xattn_bq, L0_xattn_Wk, L0_xattn_bk, L0_xattn_Wv, L0_xattn_bv, L0_xattn_Wo, L0_xattn_bo, L0_xattn_ln_g, L0_xattn_ln_b, L1_xattn_m_norm_w, L1_xattn_in_proj_w, L1_xattn_conv_w, L1_xattn_conv_b, L1_xattn_dt_bias, L1_xattn_A_log, L1_xattn_D_skip, L1_xattn_gnorm_w, L1_xattn_out_proj_w, L1_xattn_ca_ln_w, L1_xattn_ca_ln_b, L1_xattn_Wq, L1_xattn_Wk, L1_xattn_Wv, L1_xattn_Wo):
    import jax
    import jax.numpy as jnp

    def _L0_xattn_ref(query, key, value, mask, Wq, bq, Wk, bk, Wv, bv, Wo, bo, ln_g, ln_b):
        import jax, jax.numpy as jnp
        import numpy as np
        H = 256
        NH = 16
        HD = H // NH
        EPS = 1e-05

        def _split_heads(x, B, L):
            return x.reshape(B, L, NH, HD).transpose(0, 2, 1, 3)
        B, LQ, _ = query.shape
        LK = key.shape[1]
        Q = _split_heads(query @ Wq.T + bq, B, LQ)
        K = _split_heads(key @ Wk.T + bk, B, LK)
        V = _split_heads(value @ Wv.T + bv, B, LK)
        scores = jnp.einsum('bhqd,bhkd->bhqk', Q, K) / np.sqrt(HD)
        scores = jnp.where(mask[:, None, :, :] == 0, jnp.float32(-1000000000.0), scores)
        attn = jax.nn.softmax(scores, axis=-1)
        ctx = jnp.einsum('bhqk,bhkd->bhqd', attn, V)
        ctx = ctx.transpose(0, 2, 1, 3).reshape(B, LQ, H)
        out = ctx @ Wo.T + bo
        x = out + query
        mu = jnp.mean(x, axis=-1, keepdims=True)
        var = jnp.mean(jnp.square(x - mu), axis=-1, keepdims=True)
        return (x - mu) / jnp.sqrt(var + EPS) * ln_g + ln_b

    def _L1_xattn_ref(x, encoder_out, encoder_padding_mask, m_norm_w, in_proj_w, conv_w, conv_b, dt_bias, A_log, D_skip, gnorm_w, out_proj_w, ca_ln_w, ca_ln_b, Wq, Wk, Wv, Wo):
        import jax, jax.numpy as jnp
        import numpy as np
        D = 256
        D_STATE = 128
        N_HEADS = 8
        D_INNER = 2 * D
        HEADDIM = 64
        H_M = D_INNER // HEADDIM
        D_CONV = 4
        CONV_DIM = D_INNER + 2 * D_STATE
        D_IN_PROJ = 2 * D_INNER + 2 * D_STATE + H_M
        B = 1
        LQ = 256
        LK = 512
        EPS = 1e-05

        def _rms(x, w):
            return x * jax.lax.rsqrt(jnp.mean(x * x, axis=-1, keepdims=True) + EPS) * w

        def _ln(x, w, b):
            mu = jnp.mean(x, axis=-1, keepdims=True)
            v = jnp.mean((x - mu) ** 2, axis=-1, keepdims=True)
            return (x - mu) * jax.lax.rsqrt(v + EPS) * w + b

        def _mamba2_block(x, norm_w, in_proj_w, conv_w, conv_b, dt_bias, A_log, D_skip, gnorm_w, out_proj_w):
            b, L, _ = x.shape
            resid = x
            zxbcdt = _rms(x, norm_w) @ in_proj_w
            z = zxbcdt[..., :D_INNER]
            xBC = zxbcdt[..., D_INNER:D_INNER + CONV_DIM]
            dt = jax.nn.softplus(zxbcdt[..., -H_M:] + dt_bias)
            padded = jnp.pad(xBC, ((0, 0), (D_CONV - 1, 0), (0, 0)))
            conv = conv_b + sum((padded[:, k:k + L, :] * conv_w[:, k] for k in range(D_CONV)))
            xBC = jax.nn.silu(conv)
            xh = xBC[..., :D_INNER].reshape(b, L, H_M, HEADDIM)
            Bm = xBC[..., D_INNER:D_INNER + D_STATE]
            Cm = xBC[..., D_INNER + D_STATE:]
            A = -jnp.exp(A_log)
            decay = jnp.exp(dt * A)
            dbx = dt[..., None] * xh

            def step(h, inp):
                dec, u, bt, ct = inp
                h = h * dec[:, :, None, None] + u[..., None] * bt[:, None, None, :]
                y = jnp.einsum('bhpn,bn->bhp', h, ct)
                return (h, y)
            h0 = jnp.zeros((b, H_M, HEADDIM, D_STATE), x.dtype)
            xs = (decay.transpose(1, 0, 2), dbx.transpose(1, 0, 2, 3), Bm.transpose(1, 0, 2), Cm.transpose(1, 0, 2))
            _, ys = jax.lax.scan(step, h0, xs)
            y = ys.transpose(1, 0, 2, 3) + D_skip[None, None, :, None] * xh
            u = _rms(y.reshape(b, L, D_INNER) * jax.nn.silu(z), gnorm_w)
            return resid + u @ out_proj_w

        def _cross_attention(x, enc, pad_mask, ln_w, ln_b, Wq, Wk, Wv, Wo):
            b, Lq, _ = x.shape
            Lk = enc.shape[1]
            dh = D // N_HEADS
            resid = x
            xn = _ln(x, ln_w, ln_b)
            q = (xn @ Wq).reshape(b, Lq, N_HEADS, dh)
            k = (enc @ Wk).reshape(b, Lk, N_HEADS, dh)
            v = (enc @ Wv).reshape(b, Lk, N_HEADS, dh)
            scores = jnp.einsum('bqhd,bkhd->bhqk', q, k) * np.float32(1.0 / np.sqrt(dh))
            scores = jnp.where(pad_mask[:, None, None, :], jnp.float32(-1000000000.0), scores)
            p = jax.nn.softmax(scores, axis=-1)
            ctx = jnp.einsum('bhqk,bkhd->bqhd', p, v).reshape(b, Lq, D)
            return resid + ctx @ Wo
        h = _mamba2_block(x, m_norm_w, in_proj_w, conv_w, conv_b, dt_bias, A_log, D_skip, gnorm_w, out_proj_w)
        return _cross_attention(h, encoder_out, encoder_padding_mask, ca_ln_w, ca_ln_b, Wq, Wk, Wv, Wo)
    x = _L0_xattn_ref(x, ctx_1024, ctx_1024, mask_BxSxS2_ik1, L0_xattn_Wq, L0_xattn_bq, L0_xattn_Wk, L0_xattn_bk, L0_xattn_Wv, L0_xattn_bv, L0_xattn_Wo, L0_xattn_bo, L0_xattn_ln_g, L0_xattn_ln_b)
    x = _L1_xattn_ref(x, ctx_1024, mask_1xS2_bf0, L1_xattn_m_norm_w, L1_xattn_in_proj_w, L1_xattn_conv_w, L1_xattn_conv_b, L1_xattn_dt_bias, L1_xattn_A_log, L1_xattn_D_skip, L1_xattn_gnorm_w, L1_xattn_out_proj_w, L1_xattn_ca_ln_w, L1_xattn_ca_ln_b, L1_xattn_Wq, L1_xattn_Wk, L1_xattn_Wv, L1_xattn_Wo)
    return x

_drawn_inputs = setup_inputs


def setup_inputs(seed=0):
    import zlib

    import numpy as np

    out = dict(_drawn_inputs(seed))
    spreads = {'L0_xattn_bq': (0.0, 0.401),
     'L0_xattn_bk': (0.0, 0.8),
     'L0_xattn_bv': (0.0, 0.1),
     'L0_xattn_bo': (0.0, 0.1),
     'L0_xattn_ln_g': (1.0, 0.2),
     'L0_xattn_ln_b': (0.0, 0.1),
     'L1_xattn_m_norm_w': (1.0, 0.2),
     'L1_xattn_conv_b': (0.0, 0.1),
     'L1_xattn_dt_bias': (-4.600165843963623, 0.6),
     'L1_xattn_D_skip': (1.0, 0.2),
     'L1_xattn_gnorm_w': (1.0, 0.2),
     'L1_xattn_ca_ln_w': (1.0, 0.6),
     'L1_xattn_ca_ln_b': (0.0, 0.8)}
    factors = {'L1_xattn_A_log': 8.0, 'L1_xattn_Wq': 8.0, 'L1_xattn_Wk': 8.0}
    for name, (base, spread) in spreads.items():
        noise = np.random.default_rng([zlib.crc32(name.encode()), seed]).standard_normal(out[name].shape)
        drawn = base * np.exp(spread * noise) if base else spread * noise
        out[name] = jnp.asarray(drawn.astype(out[name].dtype))
    for name, factor in factors.items():
        out[name] = (out[name] * factor).astype(out[name].dtype)
    return out
```

```python
from contextlib import ExitStack

import concourse.bass as bass
from concourse import mybir

F32 = mybir.dt.float32
F32R = mybir.dt.float32r
BF16 = mybir.dt.bfloat16
I32 = mybir.dt.int32
U8 = mybir.dt.uint8
ALU = mybir.AluOpType
ACT = mybir.ActivationFunctionType
AX = mybir.AxisListType

P = 128
H0, HD0 = 16, 16
H1, HD1 = 8, 32
GH = 4
G0, G1 = H0 // GH, H1 // GH
NG = G0 + G1
HM, PD, NS = 8, 64, 128
DI = HM * PD
TAPS = 4
MASKED = -(2.0 ** 100)
PADDED = -(2.0 ** 120)
EPS = 1e-5
ATANH = [1.0 / n for n in (17, 15, 13, 11, 9, 7, 5, 3)]


def xattn_mamba(nc, x, xt, ctxt, mask, maskt, mask1, wq0, bq0, wk0, bk0, wv0, bv0, wo0, bo0, ln_g, ln_b,
                norm_w, w_in, conv_w, conv_b, dt_bias, a_log, d_skip, gnorm_w, w_out, ca_w, ca_b,
                wq1, wk1, wv1, wo1, out):
    B, T, D = x.shape
    S = ctxt.shape[2]
    QT = T // P
    DT = D // P
    KT = -(-S // P)
    SP = KT * P
    LAST = S - (KT - 1) * P
    SE = S + S % 2
    NCHUNK = -(-SE // 512)
    CW = -(-SE // (2 * NCHUNK)) * 2
    CHUNKS = [(c, min(CW, SE - c)) for c in range(0, SE, CW)]
    KCH = [(c, min(CW, S - c)) for c in range(0, S, CW)]
    NC = len(CHUNKS)
    VW = HD0 + 1
    VROW = H0 * VW + 32 - VW
    RAW = GH * QT * NC + 1
    NPJ0 = DT + NC + KT + NC
    NPJ = 2 * NPJ0
    NPIECE = QT * NC + KT + 1
    NCH = 2 * DI // P // 2 + 2
    XT = DI // P
    DCONST = 22
    LEAD = 1
    NLOAD = 26
    SPN = 7 + len(ATANH) + 2
    CORDER = [XT, XT + 1] + list(range(XT))

    with ExitStack() as ctx:
        def sb(name, shape, dt):
            return ctx.enter_context(nc.sbuf_tensor(name, shape, dt))

        def sem(name):
            return ctx.enter_context(nc.semaphore(name))

        wq0_s = sb("wq0_s", [P, DT, D], F32)
        wk0_s = sb("wk0_s", [P, DT, D], F32)
        wv0_s = sb("wv0_s", [P, DT, D], F32)
        wo0_s = sb("wo0_s", [P, G0, D], F32)
        wq1_s = sb("wq1_s", [P, DT, D], F32)
        wk1_s = sb("wk1_s", [P, DT, D], F32)
        wv1_s = sb("wv1_s", [P, DT, D], F32)
        wo1_s = sb("wo1_s", [P, G1, D], F32)
        win_s = sb("win_s", [P, DT, w_in.shape[1]], F32)
        wout_s = sb("wout_s", [P, XT, D], F32)
        bv_s = sb("bv_s", [P, D], F32)
        bo_s = sb("bo_s", [P, D], F32)
        lng_s = sb("lng_s", [P, D], F32)
        lnb_s = sb("lnb_s", [P, D], F32)
        cols = sb("cols", [P, 96], F32)
        bq_c, bk_c = cols[:, 0:2], cols[:, 2:4]
        nw_c, caw_c, cab_c = cols[:, 4:6], cols[:, 6:8], cols[:, 8:10]
        gw_c = cols[:, 10:14]
        dsk_c = cols[:, 14:18]
        cb_c = cols[:, 18:24]
        cw_c = cols[:, 24:48]
        dtb_c, a_c = cols[:, 48:56], cols[:, 56:64]
        keep1_c = cols[:, 64:65]
        small = sb("small", [P, 4], F32)
        ident = sb("ident", [P, P], F32)
        identb = sb("identb", [P, P], BF16)
        upto = sb("upto", [P, P], F32)
        after = sb("after", [P, P], F32)
        ones = sb("ones", [P, P], F32)
        pick = sb("pick", [P, P], F32)
        neghalf = sb("neghalf", [P, 4], F32)
        ctxs = sb("ctxs", [P, DT, S], F32)
        KS = [sb(f"KS{i}", [P, GH, SP], F32R) for i in range(2)]
        QS = [sb(f"QS{i}", [P, GH, T], F32R) for i in range(2)]
        xres = sb("xres", [P, QT, D], F32)
        vbuf = sb("vbuf", [P, KT * VROW], F32)
        v0 = vbuf[:, :].rearrange("p (k c) -> p k c", k=KT)
        v1 = vbuf[:, 0:KT * D].rearrange("p (k c) -> p k c", k=KT)
        khl = sb("khl", [P, 2, SE], F32R)
        stage = sb("stage", [P, 2, 512], I32)
        mx = sb("mx", [P, NC, 16], F32)
        mxr = sb("mxr", [P, 16], F32)
        nm = sb("nm", [P, 32], F32R)
        mrow = [sb(f"mrow{i}", [32, P], F32R) for i in range(2)]
        stats = sb("stats", [P, QT, 6], F32)
        moments = sb("moments", [P, QT, 2], F32)
        rstd = sb("rstd", [P, 3, QT], F32)

        base = nc.sbuf_base if isinstance(nc.sbuf_base, int) else nc.sbuf_base()
        base = -(-base // 32) * 32
        place = [base]

        def at(name, shape, dt):
            n = 1
            for s in shape[1:]:
                n *= s
            off = place[0]
            place[0] += -(-n * (2 if dt is BF16 else 4) // 32) * 32
            return nc.alloc_sbuf_tensor_at(name, shape, dt, offset=off)

        PR = at("PR", [P, 2, GH, T], F32)
        maskq = at("maskq", [P, QT, SE], BF16)
        maskk = at("maskk", [P, KT, T], BF16)
        qhl = at("qhl", [P, DT, 2, T], F32R)
        ctxn = at("ctxn", [P, G0, T], F32)
        rs = at("rs", [P, T], F32)
        top_attention = place[0]
        xt_s = ctxn[:, G1:G1 + DT, :]
        place[0] = base
        xc = at("xc", [P, NCH, T], F32)
        zs = at("zs", [P, XT, T], F32)
        yt = at("yt", [P, XT, T], F32)
        xs = yt[:, 0:2, :].rearrange("p a (b d) -> p (a b) d", d=D)
        xn = at("xn", [P, DT, T], F32)
        rawc = at("rawc", [P, 2, T + TAPS], F32)
        th = at("th", [P, 2, T], F32)
        aU = at("aU", [P, HM, P], F32)
        Ld = at("Ld", [P, HM, P], F32)
        Ce = at("Ce", [P, HM, P], F32)
        Hst = at("Hst", [P, DI], F32)
        dx = at("dx", [P, DI], F32)
        dx2 = at("dx2", [P, DI], F32)
        btok = at("btok", [P, P], F32)
        GM = at("GM", [P, P], F32)
        sp_t = at("sp_t", [P, 8, QT * HM], F32)
        dtt = at("dtt", [P, QT, HM], F32)
        aa = at("aa", [P, QT, HM], F32)
        dec = at("dec", [P, 2, QT * HM], F32)
        top = max(top_attention, place[0])
        assert top <= nc.sbuf_usable_end, (top, nc.sbuf_usable_end)
        xs1 = xc[:, 0:2, :].rearrange("p a (b d) -> p (a b) d", d=D)
        zero_rows = PR[0:33, 0, :, :].rearrange("p h t -> p (h t)")
        one_row = PR[0:1, 1, :, :].rearrange("p h t -> p (h t)")
        mask1_s = PR[:, :, :, :].rearrange("p a h t -> p (a h t)").bitcast(U8)[:, 0:S]
        m1row = ctxn[0:1, :, :].rearrange("p g t -> p (g t)")[:, 0:SP]
        zsrc = nc.dram_tensor("const_rows", (34, GH * T), F32, kind="Internal").ap()

        ps = ctx.enter_context(nc.psum_tensor("ps", [P, 8, 512], F32))

        s_w = sem("s_w")
        s_const = sem("s_const")
        s_dconst = sem("s_dconst")
        s_aconst = sem("s_aconst")
        s_rows = sem("s_rows")
        s_ctx = sem("s_ctx")
        s_xt = sem("s_xt")
        s_x = sem("s_x")
        s_stage = [sem(f"s_stage{i}") for i in range(2)]
        s_conv = sem("s_conv")
        s_vfix = sem("s_vfix")
        s_proj = sem("s_proj")
        s_hi = sem("s_hi")
        s_projfree = sem("s_projfree")
        s_kst = [sem(f"s_kst{i}") for i in range(2)]
        s_qst = [sem(f"s_qst{i}") for i in range(2)]
        s_mload = [sem(f"s_mload{i}") for i in range(2)]
        s_raw = sem("s_raw")
        s_rawfree = sem("s_rawfree")
        s_mx = sem("s_mx")
        s_mhi = sem("s_mhi")
        s_nm = sem("s_nm")
        s_mrow = sem("s_mrow")
        s_s = sem("s_s")
        s_p = sem("s_p")
        s_pv = sem("s_pv")
        s_ctxn = sem("s_ctxn")
        s_sum = sem("s_sum")
        s_rs = sem("s_rs")
        s_scopy = sem("s_scopy")
        s_norm = sem("s_norm")
        s_o = sem("s_o")
        s_xb = sem("s_xb")
        s_y = sem("s_y")
        s_st = sem("s_st")
        s_mom = sem("s_mom")
        s_ve = sem("s_ve")
        s_rstd = sem("s_rstd")
        s_ln = [sem(f"s_ln{i}") for i in range(3)]
        s_sq = sem("s_sq")
        s_rm = sem("s_rm")
        s_rms = sem("s_rms")
        s_xs = sem("s_xs")
        s_xst = sem("s_xst")
        s_xn = sem("s_xn")
        s_in = sem("s_in")
        s_sp = sem("s_sp")
        s_spe = sem("s_spe")
        s_a = sem("s_a")
        s_pad = sem("s_pad")
        s_rawcp = sem("s_rawcp")
        s_cv = sem("s_cv")
        s_conv4 = sem("s_conv4")
        s_th = sem("s_th")
        s_xc = sem("s_xc")
        s_zth = sem("s_zth")
        s_zs = sem("s_zs")
        s_dps = sem("s_dps")
        s_dec = sem("s_dec")
        s_au = sem("s_au")
        s_D = sem("s_D")
        s_Ld = sem("s_Ld")
        s_cum = sem("s_cum")
        s_Ecb = sem("s_Ecb")
        s_G = sem("s_G")
        s_GM = sem("s_GM")
        s_M = sem("s_M")
        s_CE = sem("s_CE")
        s_tok = sem("s_tok")
        s_bt = sem("s_bt")
        s_btok = sem("s_btok")
        s_dx = sem("s_dx")
        s_dx2 = sem("s_dx2")
        s_yp = sem("s_yp")
        s_yt = sem("s_yt")
        s_hp = sem("s_hp")
        s_hs = sem("s_hs")
        s_h = sem("s_h")
        s_g = sem("s_g")
        s_g2 = sem("s_g2")
        s_op = sem("s_op")
        s_ssq = sem("s_ssq")
        s_gr1 = sem("s_gr1")
        s_gr2 = sem("s_gr2")
        s_gr = sem("s_gr")
        s_blk = sem("s_blk")
        s_st1 = sem("s_st1")
        s_mom1 = sem("s_mom1")
        s_ve1 = sem("s_ve1")
        s_rstd1 = sem("s_rstd1")
        s_xs1 = sem("s_xs1")
        s_xst1 = sem("s_xst1")
        s_xn1 = sem("s_xn1")
        s_fin = sem("s_fin")
        s_out = sem("s_out")

        f = lambda a: a.bitcast(F32)

        def alone(eng):
            eng.nop(nofuse=True)

        PJ = []
        for layer in range(2):
            q = [(layer, "q", i) for i in range(DT)]
            k = [[(layer, "k", (i, c)) for c in range(NC)] for i in range(DT)]
            v = [(layer, "v", i) for i in range(KT)]
            if layer == 0:
                steps = [[item] for item in v]
                for c, item in enumerate(k[1]):
                    steps[KT - 1 - 2 * (NC - c)].append(item)
                FRONT = q + k[0]
                PJ += FRONT + [item for s in steps for item in s]
            else:
                PJ += k[0] + v + k[1] + q
        pj_index = {item: n for n, item in enumerate(PJ)}
        hi_index = {}
        for item in PJ:
            if item[1] != "v":
                hi_index[item] = len(hi_index)
        NHI = len(hi_index)
        SECOND = PJ[NPJ0:NPJ - DT]
        LASTQ = PJ[NPJ - DT:]
        pj_bank = {}
        for n, item in enumerate(FRONT):
            pj_bank[item] = n % 4
        for s in steps:
            for item in s:
                pj_bank[item] = 7
        for n, item in enumerate(SECOND):
            pj_bank[item] = 6 + n % 2
        for n, item in enumerate(LASTQ):
            pj_bank[item] = n % 2
        pj_before = {}
        last_in = {}
        for item in PJ:
            pj_before[item] = last_in.get((item in FRONT, pj_bank[item]))
            last_in[(item in FRONT, pj_bank[item])] = item

        KCUM = [G0 * 16, 2 * G0 * 16, 2 * G0 * 16 + 48]
        QCUM = [80, 160, 224]
        KPER, QPER, MPER = KCUM[-1], QCUM[-1], 96

        PIECES = [(0, i, c, n) for i in range(QT) for c, n in KCH]
        PIECES += [(1, i, 0, T) for i in range(KT - 1)] + [(1, KT - 1, 0, T // 2), (1, KT - 1, T // 2, T // 2)]
        assert len(PIECES) == NPIECE and NPIECE % 2 == 0
        HALF = NPIECE // 2
        PIECE1, PIECE2 = QT * NC + 4, NPIECE - 8

        def piece_dram(b, piece):
            kind, i, c, n = piece
            if kind == 0:
                return mask[b, i * P:(i + 1) * P, c:c + n], P, n
            rows = P if i < KT - 1 else LAST
            return maskt[b, i * P:i * P + rows, c:c + n], rows, n

        SLOTS = 6

        def raw_after(step, slot):
            n = RAW - 1
            lo, hi = 1, KT - 3
            if step < lo or step > hi:
                return range(0)
            w, at_slot = (hi - lo + 1) * SLOTS, (step - lo) * SLOTS + slot
            return range(n * at_slot // w, n * (at_slot + 1) // w)

        FEVERY = (RAW - 1) // (len(FRONT) + 1)

        block = ctx.enter_context(nc.Block())

        @block.sync
        def _(sp):
            nload = 0
            for dst, src in (
                (wq0_s[:, :, :], wq0.rearrange("(k p) n -> p k n", p=P)),
                (wk0_s[:, :, :], wk0.rearrange("(k p) n -> p k n", p=P)),
                (wv0_s[:, :, :], wv0.rearrange("(k p) n -> p k n", p=P)),
                (wq1_s[:, :, :], wq1.rearrange("(k p) n -> p k n", p=P)),
                (wk1_s[:, :, :], wk1.rearrange("(k p) n -> p k n", p=P)),
                (wv1_s[:, :, :], wv1.rearrange("(k p) n -> p k n", p=P)),
                (wo1_s[:, :, :], wo1.rearrange("(k p) n -> p k n", p=P)),
                (win_s[:, :, :], w_in.rearrange("(k p) n -> p k n", p=P)),
                (wout_s[:, :, :], w_out.rearrange("(k p) n -> p k n", p=P)),
                (bv_s[:, :], bv0.unsqueeze(0).broadcast_to([P, D])),
                (bo_s[:, :], bo0.unsqueeze(0).broadcast_to([P, D])),
                (lng_s[:, :], ln_g.unsqueeze(0).broadcast_to([P, D])),
                (lnb_s[:, :], ln_b.unsqueeze(0).broadcast_to([P, D])),
                (cw_c.rearrange("p (i k) -> p i k", k=TAPS), conv_w.rearrange("(i p) k -> p i k", p=P)),
                (dtb_c, dt_bias.unsqueeze(0).broadcast_to([P, HM])),
                (a_c, a_log.unsqueeze(0).broadcast_to([P, HM])),
            ):
                sp.dma_start(dst, src).then_inc(s_w, 16)
                nload += 1
            with nc.allow_non_contiguous_dma(reason="per-channel columns, once"):
                for dst, src in ((bq_c, bq0), (bk_c, bk0), (nw_c, norm_w), (caw_c, ca_w), (cab_c, ca_b),
                                 (gw_c, gnorm_w), (cb_c, conv_b)):
                    sp.dma_start(dst, src.rearrange("(i p) -> p i", p=P)).then_inc(s_w, 16)
                    nload += 1
                for half in range(2):
                    sp.dma_start(dsk_c[half * PD:(half + 1) * PD, :],
                                 d_skip.rearrange("(i e) -> e i", e=2)[half:half + 1, :]
                                 .broadcast_to([PD, XT])).then_inc(s_w, 16)
                    nload += 1
            sp.dma_start(mask1_s, mask1.broadcast_to([P, S])).then_inc(s_w, 16)
            nload += 1
            assert nload == NLOAD, nload
            sp.wait_ge(s_const, 1)
            for j in range(GH):
                sp.dma_start(wo0_s[32 * j:32 * j + HD0, :, :],
                             wo0.rearrange("(g j d) n -> j d g n", j=GH, d=HD0)[j]).then_inc(s_w, 16)
            sp.wait_ge(s_dconst, DCONST)
            sp.dma_start(zsrc[0:33, :], zero_rows).then_inc(s_rows, 16)
            sp.dma_start(zsrc[33:34, :], one_row).then_inc(s_rows, 16)
            for i in range(2):
                for j in range(GH):
                    sp.dma_start(f(KS[i][96:97, j, :]), m1row).then_inc(s_rows, 16)
            sp.wait_ge(s_rows, 160)

            def load_pieces(b, bnext, lo, hi, first):
                for n in range(lo, hi):
                    src, rows, w = piece_dram(bnext, PIECES[n])
                    if not first or n >= 2:
                        sp.wait_ge(s_conv, n - 1 if first else (b + 1) * NPIECE + n - 1)
                        alone(sp)
                    sp.dma_start(stage[0:rows, n % 2, 0:w], src).then_inc(s_stage[n % 2], 16)

            def load_ctx(bnext):
                sp.dma_start(ctxs[:, :, :], ctxt[bnext].rearrange("(k p) n -> p k n", p=P)).then_inc(s_ctx, 16)

            def load_xt(bnext):
                sp.dma_start(xt_s, xt[bnext].rearrange("(k p) n -> p k n", p=P)).then_inc(s_xt, 16)

            def stack_k(gi):
                slot, dst = gi % 2, KS[gi % 2]
                if gi < G0:
                    p0 = 64 * (gi % 2)
                    for n, part in enumerate((0, 1, 0, 1)):
                        sp.dma_start(f(dst[16 * n:16 * n + 16, :, 0:S]),
                                     f(khl[p0:p0 + 64, part, 0:S])).then_inc(s_kst[slot], 16)
                else:
                    for n, part in enumerate((0, 1, 0)):
                        sp.dma_start(f(dst[32 * n:32 * n + 32, :, 0:S]),
                                     f(khl[:, part, 0:S])).then_inc(s_kst[slot], 16)

            def stack_q(gi):
                slot, dst = gi % 2, QS[gi % 2]
                if gi < G0:
                    p0 = 64 * (gi % 2)
                    for n, part in enumerate((0, 0, 1, 1)):
                        sp.dma_start(f(dst[16 * n:16 * n + 16, :, :]),
                                     f(qhl[p0:p0 + 64, gi // 2, part, :])).then_inc(s_qst[slot], 16)
                    sp.dma_start(f(dst[64:97, :, :]), zsrc[0:33, :].rearrange("p (h t) -> p h t", h=GH))\
                        .then_inc(s_qst[slot], 16)
                else:
                    for n, part in enumerate((0, 0, 1)):
                        sp.dma_start(f(dst[32 * n:32 * n + 32, :, :]),
                                     f(qhl[:, gi - G0, part, :])).then_inc(s_qst[slot], 16)
                    sp.dma_start(f(dst[96:97, :, :]), zsrc[33:34, :].rearrange("p (h t) -> p h t", h=GH))\
                        .then_inc(s_qst[slot], 16)

            def maxima_row(b, gi):
                sp.wait_ge(s_mrow, b * NG + gi + 1)
                alone(sp)
                for part in range(2):
                    sp.dma_start(f(QS[gi % 2][97 + part:98 + part, :, :]),
                                 f(mrow[gi % 2][16 * part:16 * part + 16, :])).then_inc(s_mload[gi % 2], 16)

            for first in (*s_kst, *s_qst, *s_mload, s_out):
                sp.nop(nofuse=True).then_inc(first, LEAD)
            load_ctx(0)
            load_xt(0)
            load_pieces(None, 0, 0, NPIECE, True)
            sp.wait_ge(s_projfree, len(FRONT))
            stack_k(0)
            stack_q(0)
            maxima_row(0, 0)
            with sp.Fori(0, B) as b:
                bn = (b + 1) % B
                sp.wait_ge(s_out, LEAD + b * 16 * QT)
                alone(sp)
                sp.dma_start(xres[:, :, :], x[b].rearrange("(i p) d -> p i d", p=P)).then_inc(s_x, 16)
                sp.wait_ge(s_pv, LEAD + b * NG * KT)
                alone(sp)
                stack_k(1)
                stack_q(1)
                maxima_row(b, 1)
                for gi in range(2, G0):
                    sp.wait_ge(s_pv, LEAD + b * NG * KT + (gi - 1) * KT)
                    alone(sp)
                    sp.wait_ge(s_projfree, b * NPJ + pj_index[(0, "k", (1, NC - 1))] + 1)
                    alone(sp)
                    stack_k(gi)
                    stack_q(gi)
                    maxima_row(b, gi)
                for g in range(G1):
                    gi = G0 + g
                    sp.wait_ge(s_pv, LEAD + b * NG * KT + (gi - 1) * KT)
                    alone(sp)
                    sp.wait_ge(s_projfree, b * NPJ + pj_index[(1, "k", (g, NC - 1))] + 1)
                    alone(sp)
                    stack_k(gi)
                load_ctx(bn)
                sp.wait_ge(s_projfree, b * NPJ + NPJ)
                alone(sp)
                load_xt(bn)
                for g in range(G1):
                    stack_q(G0 + g)
                load_pieces(b, bn, 0, PIECE1, False)
                maxima_row(b, G0)
                load_pieces(b, bn, PIECE1, PIECE2, False)
                maxima_row(b, G0 + 1)
                sp.wait_ge(s_pv, LEAD + b * NG * KT + (G0 + 1) * KT)
                alone(sp)
                sp.wait_ge(s_projfree, (b + 1) * NPJ + len(FRONT))
                alone(sp)
                stack_k(0)
                stack_q(0)
                load_pieces(b, bn, PIECE2, NPIECE, False)
                maxima_row(b + 1, 0)
                for i in range(QT):
                    sp.wait_ge(s_fin, LEAD + b * QT + i + 1)
                    alone(sp)
                    sp.dma_start(out[b, i * P:(i + 1) * P, :], xres[:, i, :]).then_inc(s_out, 16)
            sp.wait_ge(s_out, LEAD + B * QT * 16)
            sp.wait_ge(s_ctx, (B + 1) * 16)
            sp.wait_ge(s_xt, (B + 1) * 16)
            sp.wait_ge(s_mload[0], LEAD + B * MPER + 32)

        @block.gpsimd
        def _(pool):
            nc.gpsimd.memset(wo0_s[:, :, :], 0.0).then_inc(s_const, 1)
            nc.gpsimd.memset(ident[:, :], 0.0).then_inc(s_const, 1)
            nc.gpsimd.memset(ones[:, :], 1.0).then_inc(s_const, 1)
            nc.gpsimd.memset(pick[:, :], 0.0).then_inc(s_const, 1)
            nc.gpsimd.memset(neghalf[:, :], -0.5).then_inc(s_const, 1)
            pool.wait_ge(s_const, 5)
            nc.gpsimd.affine_select(out=ident[:, :], in_=ident[:, :], compare_op=ALU.not_equal, fill=1.0, base=0,
                                    pattern=[[-1, P]], channel_multiplier=1).then_inc(s_const, 1)
            nc.gpsimd.affine_select(out=upto[:, :], in_=ones[:, :], compare_op=ALU.is_ge, fill=0.0, base=0,
                                    pattern=[[1, P]], channel_multiplier=-1).then_inc(s_const, 1)
            nc.gpsimd.affine_select(out=after[:, :], in_=ones[:, :], compare_op=ALU.is_gt, fill=0.0, base=0,
                                    pattern=[[-1, P]], channel_multiplier=1).then_inc(s_const, 1)
            pv = pick[:, :].rearrange("p (j r) -> p j r", j=GH)
            nc.gpsimd.affine_select(out=pv, in_=pv, compare_op=ALU.not_equal, fill=1.0, base=-HD0,
                                    pattern=[[-32, GH], [0, 32]], channel_multiplier=1).then_inc(s_const, 1)

            def convert(n, count):
                kind, i, c, w = PIECES[n]
                rows = P if kind == 0 or i < KT - 1 else LAST
                dst = maskq[:, i, c:c + w] if kind == 0 else maskk[0:rows, i, c:c + w]
                pool.wait_ge(s_stage[n % 2], count)
                alone(pool)
                nc.gpsimd.tensor_scalar(dst, stage[0:rows, n % 2, 0:w], 0.0, MASKED, ALU.is_equal, ALU.mult)\
                    .then_inc(s_conv, 1)

            def pad_masks():
                nc.gpsimd.memset(maskq[:, :, S:SE], PADDED)
                nc.gpsimd.memset(maskk[:, KT - 1, :], PADDED).then_inc(s_vfix, 1)

            pool.wait_ge(s_rows, 160)
            pad_masks()
            pool.wait_ge(s_vfix, 1)
            for n in range(NPIECE):
                convert(n, 16 * (n // 2 + 1))
            with pool.Fori(0, B) as b:
                pool.wait_ge(s_pv, LEAD + b * NG * KT)
                alone(pool)
                nc.gpsimd.memset(v0[:, :, 0:H0 * VW].rearrange("p k (h c) -> p k h c", c=VW)[:, :, :, HD0:VW], 1.0)
                nc.gpsimd.memset(v0[:, :, H0 * VW:VROW], 0.0).then_inc(s_vfix, 1)
                pool.wait_ge(s_x, 16 * (b + 1))
                for i in range(QT):
                    nc.gpsimd.tensor_tensor(xres[:, i, :], xres[:, i, :], bo_s[:, :], ALU.add).then_inc(s_xb, 1)
                pool.wait_ge(s_mom, QT * (b + 1))
                alone(pool)
                nc.gpsimd.tensor_scalar(rstd[:, 0, :], moments[:, :, 1], EPS, 1.0, ALU.add, ALU.mult).then_inc(s_ve, 1)
                pool.wait_ge(s_ve, b + 1)
                nc.gpsimd.tensor_tensor(rstd[:, 0, :], rstd[:, 0, :], neghalf[:, :], ALU.pow).then_inc(s_rstd, 1)
                pool.wait_ge(s_pv, LEAD + b * NG * KT + G0 * KT)
                alone(pool)
                for i in range(2):
                    ins = nc.gpsimd.memset(rawc[:, i, 0:TAPS - 1], 0.0)
                ins.then_inc(s_pad, 1)
                pool.wait_ge(s_sq, QT * (b + 1))
                alone(pool)
                nc.gpsimd.tensor_scalar(rstd[:, 1, :], stats[:, :, 0], 1.0 / D, EPS, ALU.mult, ALU.add)\
                    .then_inc(s_rm, 1)
                pool.wait_ge(s_rm, b + 1)
                nc.gpsimd.tensor_tensor(rstd[:, 1, :], rstd[:, 1, :], neghalf[:, :], ALU.pow).then_inc(s_rms, 1)
                pool.wait_ge(s_a, b + 1)
                for c in range(QT):
                    if c > 0:
                        pool.wait_ge(s_D, b * QT + c)
                        if c > 1:
                            pool.wait_ge(s_cum, b * (QT - 1) + c - 1)
                    nc.gpsimd.tensor_tensor(
                        aU[:, :, :], aa[:, c, :].unsqueeze(2).broadcast_to([P, HM, P]),
                        upto[:, :].unsqueeze(1).broadcast_to([P, HM, P]), ALU.mult).then_inc(s_au, 1)
                    if c > 0:
                        pool.wait_ge(s_Ecb, b * (QT - 1) + c)
                        nc.gpsimd.tensor_tensor(
                            Ce[:, :, :], Ce[:, :, :],
                            xc[:, NCH - 1, c * P:(c + 1) * P].unsqueeze(1).broadcast_to([P, HM, P]), ALU.mult)\
                            .then_inc(s_CE, 1)
                    if c < QT - 1:
                        pool.wait_ge(s_dx, b * QT + c + 1)
                        pool.wait_ge(s_dec, b + 1)
                        if c > 0:
                            pool.wait_ge(s_hp, b * (QT - 1) + c)
                        nc.gpsimd.tensor_tensor(
                            dx2[:, :].rearrange("p (h e) -> p h e", h=HM),
                            dx[:, :].rearrange("p (h e) -> p h e", h=HM),
                            dec[:, 0, c * HM:(c + 1) * HM].unsqueeze(2).broadcast_to([P, HM, PD]), ALU.mult)\
                            .then_inc(s_dx2, 1)
                    if 0 < c < QT - 1:
                        pool.wait_ge(s_yp, LEAD + b * QT + c + 1)
                        nc.gpsimd.tensor_tensor(
                            Hst[:, :].rearrange("p (h e) -> p h e", h=HM),
                            Hst[:, :].rearrange("p (h e) -> p h e", h=HM),
                            dec[:, 1, c * HM:(c + 1) * HM].unsqueeze(2).broadcast_to([P, HM, PD]), ALU.mult)\
                            .then_inc(s_hs, 1)
                pool.wait_ge(s_ssq, b + 1)
                alone(pool)
                nc.gpsimd.tensor_scalar(rstd[:, 1, :], stats[:, :, 0], 0.25 / DI, EPS, ALU.mult, ALU.add)\
                    .then_inc(s_gr1, 1)
                pool.wait_ge(s_gr1, b + 1)
                nc.gpsimd.tensor_tensor(rstd[:, 1, :], rstd[:, 1, :], neghalf[:, :], ALU.pow).then_inc(s_gr2, 1)
                pool.wait_ge(s_gr2, b + 1)
                alone(pool)
                nc.gpsimd.tensor_scalar(rstd[:, 2, :], rstd[:, 1, :], 0.5, 1.0, ALU.mult, ALU.mult).then_inc(s_gr, 1)
                pool.wait_ge(s_mom1, QT * (b + 1))
                alone(pool)
                nc.gpsimd.tensor_scalar(rstd[:, 0, :], moments[:, :, 1], EPS, 1.0, ALU.add, ALU.mult)\
                    .then_inc(s_ve1, 1)
                pool.wait_ge(s_ve1, b + 1)
                nc.gpsimd.tensor_tensor(rstd[:, 0, :], rstd[:, 0, :], neghalf[:, :], ALU.pow).then_inc(s_rstd1, 1)
                pool.wait_ge(s_projfree, b * NPJ + NPJ)
                alone(pool)
                pad_masks()
                pool.wait_ge(s_vfix, 1 + 2 * (b + 1))
                for n in range(NPIECE):
                    convert(n, (b + 1) * 16 * HALF + 16 * (n // 2 + 1))

        @block.tensor
        def _(pe):
            pe.wait_ge(s_w, 16 * (NLOAD + GH))
            pe.wait_ge(s_const, 9)
            pe.wait_ge(s_dconst, DCONST)
            pe.wait_ge(s_rows, 160)

            def project(b, item):
                layer, kind, i = item
                n, bank = pj_index[item], pj_bank[item]
                if pj_before[item] is not None:
                    pe.wait_ge(s_projfree, b * NPJ + pj_index[pj_before[item]] + 1)
                for k in range(DT):
                    if kind == "q":
                        o = ps[:, bank, 0:T]
                        l = (wq0_s, wq1_s)[layer][:, k, i * P:(i + 1) * P]
                        r = (xt_s, xn)[layer][:, k, :]
                    elif kind == "k":
                        c, w = KCH[i[1]]
                        o = ps[:, bank, 0:w]
                        l = (wk0_s, wk1_s)[layer][:, k, i[0] * P:(i[0] + 1) * P]
                        r = ctxs[:, k, c:c + w]
                    else:
                        rows = P if i < KT - 1 else LAST
                        o = ps[0:rows, bank, 0:D]
                        l = ctxs[:, k, i * P:i * P + rows]
                        r = (wv0_s, wv1_s)[layer][:, k, :]
                    mm = pe.matmul(o, l, r, start=(k == 0), stop=(k == DT - 1))
                mm.then_inc(s_proj, 1)

            def raw_scores(b, gi, k):
                idx = gi * RAW + k
                if k == 0:
                    pe.wait_ge(s_kst[gi % 2], LEAD + b * KPER + KCUM[gi // 2])
                    pe.wait_ge(s_qst[gi % 2], LEAD + b * QPER + QCUM[gi // 2])
                pe.wait_ge(s_rawfree, LEAD + b * NG * RAW + max(idx - 1, 0))
                h, i, c = k // (QT * NC), k // NC % QT, k % NC
                c0, w = CHUNKS[c]
                rows = 97 if gi >= G0 else 96
                pe.matmul(ps[:, 4 + idx % 2, 0:w], QS[gi % 2][0:rows, h, i * P:(i + 1) * P],
                          KS[gi % 2][0:rows, h, c0:c0 + w], start=True, stop=True).then_inc(s_raw, 1)

            def turn_maxima(b, gi):
                idx = gi * RAW + RAW - 1
                pe.wait_ge(s_rawfree, LEAD + b * NG * RAW + idx - 1)
                pe.wait_ge(s_nm, b * NG + gi + 1)
                pe.transpose(ps[0:32, 4 + idx % 2, 0:P], f(nm[:, :]), ident[:, :]).then_inc(s_raw, 1)

            def scores(b, gi, t, between):
                for half in range(2):
                    n = (gi * KT + t) * 2 + half
                    if n >= 2:
                        pe.wait_ge(s_p, b * 2 * NG * KT + n - 1)
                    for e in range(2):
                        h = 2 * half + e
                        o = ps[:, 2 * half + e, :]
                        mm = pe.matmul(o, KS[gi % 2][0:99, h, t * P:(t + 1) * P], QS[gi % 2][0:99, h, :],
                                       start=True, stop=(gi >= G0))
                        if gi < G0:
                            mm = pe.matmul(o, identb[:, :], maskk[:, t, :], start=False, stop=True)
                        if e == 1:
                            mm.then_inc(s_s, 1)
                        if gi < G0:
                            between(t, h)
                        elif h % 2 == 1:
                            between(t, h // 2)

            def times_v(b, gi, t, between):
                if t == 0:
                    if gi == G0:
                        pe.wait_ge(s_projfree, b * NPJ + NPJ)
                    else:
                        pe.wait_ge(s_ctxn, LEAD + b * NG + gi)
                    if gi > G0:
                        pe.wait_ge(s_scopy, b * G1 + gi - G0)
                if gi == 0:
                    pe.wait_ge(s_projfree, b * NPJ + pj_index[steps[t][0]] + 1)
                pe.wait_ge(s_p, b * 2 * NG * KT + (gi * KT + t + 1) * 2)
                for j in range(GH):
                    if gi < G0:
                        h = gi * GH + j
                        l = v0[:, t, h * VW:h * VW + 32]
                    else:
                        h = (gi - G0) * GH + j
                        l = v1[:, t, h * HD1:(h + 1) * HD1]
                    mm = pe.matmul(ps[32 * j:32 * j + 32, 6, :], l, PR[:, t % 2, j, :],
                                   start=(t == 0), stop=(t == KT - 1), tile_position=(0, 32 * j))
                if gi >= G0:
                    between(t + 1, 2)
                    between(t + 1, 3)
                    for j in range(GH):
                        mm = pe.matmul(ps[32 * j:32 * j + 32, 7, :], ones[:, 0:32], PR[:, t % 2, j, :],
                                       start=(t == 0), stop=(t == KT - 1), tile_position=(0, 32 * j))
                mm.then_inc(s_pv, 1)
                between(t + 1, 4)
                between(t + 1, 5)

            def spread_sums(b, g):
                pe.wait_ge(s_ctxn, LEAD + b * NG + g + 1)
                pe.wait_ge(s_projfree, b * NPJ + NPJ0)
                if g > 0:
                    pe.wait_ge(s_rs, b * NG + g)
                pe.matmul(ps[:, 7, :], pick[:, :], ctxn[:, g, :], start=True, stop=True).then_inc(s_sum, 1)

            def group(b, gi, follow):
                def between(t, slot):
                    if follow:
                        for k in raw_after(t, slot):
                            raw_scores(*follow, k)

                for t in range(KT + 1):
                    if t == 0 and 0 < gi < G0:
                        spread_sums(b, gi - 1)
                    if t == 0:
                        pe.wait_ge(s_mload[gi % 2], LEAD + b * MPER + 32 * (gi // 2 + 1))
                    if t < KT:
                        scores(b, gi, t, between)
                    if gi == 0 and t < KT:
                        project(b, steps[t][0])
                    if t >= 1:
                        times_v(b, gi, t - 1, between)
                    if gi == 0 and t < KT:
                        for item in steps[t][1:]:
                            project(b, item)
                    if follow and t == KT - 2:
                        turn_maxima(*follow)

            for first in (s_pv, s_yp):
                pe.nop(nofuse=True).then_inc(first, LEAD)

            def pass1_alone(b, gi, bf):
                front = list(FRONT)
                for k in range(RAW - 1):
                    raw_scores(b, gi, k)
                    if bf is not None and k % FEVERY == FEVERY - 1 and front:
                        if len(front) == len(FRONT):
                            pe.wait_ge(s_xt, 16 * (bf + 1))
                            pe.wait_ge(s_ctx, 16 * (bf + 1))
                        project(bf, front.pop(0))
                turn_maxima(b, gi)

            pe.wait_ge(s_xt, 16)
            pe.wait_ge(s_ctx, 16)
            for item in FRONT:
                project(0, item)
            pass1_alone(0, 0, None)
            with pe.Fori(0, B) as b:
                pe.wait_ge(s_fin, LEAD + b * QT)
                pe.wait_ge(s_conv, (b + 1) * NPIECE)
                pe.wait_ge(s_vfix, 2 + 2 * b)
                for g in range(G0):
                    group(b, g, (b, g + 1) if g + 1 < G0 else None)
                spread_sums(b, G0 - 1)
                pe.wait_ge(s_norm, LEAD + b * NG + G0)
                for i in range(QT):
                    for g in range(G0):
                        mm = pe.matmul(ps[:, i, 0:D], ctxn[:, g, i * P:(i + 1) * P], wo0_s[:, g, :],
                                       start=(g == 0), stop=(g == G0 - 1))
                    mm.then_inc(s_o, 1)

                second = list(SECOND[:NC + KT])
                late = list(SECOND[NC + KT:])

                def fill(n, items):
                    for _ in range(min(n, len(items))):
                        project(b, items.pop(0))

                pe.wait_ge(s_rs, b * NG + G0)
                fill(8, second)
                pe.wait_ge(s_y, QT * (b + 1))
                for i in range(QT):
                    pe.wait_ge(s_xs, b * QT + i + 1)
                    for k in range(DT):
                        mm = pe.transpose(ps[:, k, i * P:(i + 1) * P], xs[:, i, k * P:(k + 1) * P], ident[:, :])
                mm.then_inc(s_xst, 1)
                fill(1, second)
                pe.wait_ge(s_xn, DT * (b + 1))
                for j in range(1 + NCH + XT):
                    bank = (2 + j) % 4
                    if j == 4:
                        pe.wait_ge(s_sp, b * SPN + 1)
                    elif j >= 5:
                        pe.wait_ge(s_rawcp, b * NCH + j - 4)
                    if j == 0:
                        for i in range(QT):
                            for k in range(DT):
                                mm = pe.matmul(ps[:, bank, i * HM:(i + 1) * HM], xn[:, k, i * P:(i + 1) * P],
                                               win_s[:, k, 2 * DI + 2 * NS:2 * DI + 2 * NS + HM],
                                               start=(k == 0), stop=(k == DT - 1))
                    else:
                        c0 = DI + CORDER[j - 1] * P if j <= NCH else (j - 1 - NCH) * P
                        for k in range(DT):
                            mm = pe.matmul(ps[:, bank, :], win_s[:, k, c0:c0 + P], xn[:, k, :],
                                           start=(k == 0), stop=(k == DT - 1))
                    mm.then_inc(s_in, 1)
                pe.wait_ge(s_a, b + 1)
                pe.wait_ge(s_rawfree, LEAD + (b * NG + G0) * RAW)
                av = aa[:, :, :].rearrange("p c h -> p (c h)")
                pe.matmul(ps[:, 4, 0:QT * HM], after[:, :], av, start=True, stop=True)
                pe.matmul(ps[:, 4, QT * HM:2 * QT * HM], ones[:, :], av, start=True, stop=True).then_inc(s_dps, 1)
                for c in range(QT):
                    cs = slice(c * P, (c + 1) * P)
                    nb = b * QT + c
                    pe.wait_ge(s_au, nb + 1)
                    pe.wait_ge(s_dec, b + 1)
                    if c > 1:
                        pe.wait_ge(s_Ecb, b * (QT - 1) + c - 1)
                    elif c == 1:
                        pe.wait_ge(s_Ld, b * QT + 1)
                    for e in range(2):
                        mm = pe.matmul(ps[:, 4 + e, :], after[:, :], aU[:, 4 * e:4 * e + 4, :],
                                       start=True, stop=True)
                    mm.then_inc(s_D, 1)
                    if c == 0:
                        pe.wait_ge(s_xc, NCH * (b + 1))
                        pe.wait_ge(s_zs, XT * (b + 1))
                    if c > 0:
                        pe.wait_ge(s_dx, nb)
                        pe.wait_ge(s_btok, b * (QT - 1) + min(c, QT - 1))
                    if c > 0:
                        pe.wait_ge(s_GM, nb)
                    pe.matmul(ps[:, 1, 0:P], xc[:, NCH - 2, cs], xc[:, NCH - 1, cs], start=True, stop=True)\
                        .then_inc(s_G, 1)
                    for i in range(XT):
                        mm = pe.transpose(ps[:, 0, i * P:(i + 1) * P], xc[:, i, cs], ident[:, :])
                    mm.then_inc(s_tok, 1)
                    if c < QT - 1:
                        pe.wait_ge(s_h, LEAD + b * (QT - 1) + c)
                        pe.transpose(ps[:, 3, 0:P], xc[:, NCH - 2, cs], ident[:, :]).then_inc(s_bt, 1)
                    if c > 0:
                        pe.wait_ge(s_Ld, nb + 1)
                        for e in range(2):
                            mm = pe.matmul(ps[:, 4 + e, :], ones[:, :], aU[:, 4 * e:4 * e + 4, :],
                                           start=True, stop=True)
                        mm.then_inc(s_cum, 1)
                    fill(1, second)
                    pe.wait_ge(s_M, nb + 1)
                    pe.wait_ge(s_dx, nb + 1)
                    if c > 0:
                        pe.wait_ge(s_yt, nb * XT)
                        pe.wait_ge(s_CE, b * (QT - 1) + c)
                        pe.wait_ge(s_h, LEAD + b * (QT - 1) + c)
                    for h in range(HM):
                        i, e = h // 2, h % 2
                        o = ps[64 * e:64 * e + 64, 2, i * P:(i + 1) * P]
                        mm = pe.matmul(o, dx[:, h * PD:(h + 1) * PD], Ld[:, h, :], start=True, stop=(c == 0),
                                       tile_position=(0, 64 * e))
                        if c > 0:
                            mm = pe.matmul(o, Hst[:, h * PD:(h + 1) * PD], Ce[:, h, :], start=False, stop=True,
                                           tile_position=(0, 64 * e))
                    mm.then_inc(s_yp, 1)
                    if c < QT - 1:
                        pe.wait_ge(s_dx2, b * (QT - 1) + c + 1)
                        pe.wait_ge(s_btok, b * (QT - 1) + c + 1)
                        if c > 0:
                            pe.wait_ge(s_h, LEAD + b * (QT - 1) + c)
                        pe.matmul(ps[:, 3, :], btok[:, :], dx2[:, :], start=True, stop=True).then_inc(s_hp, 1)
                fill(len(second), second)
                fill(len(late), late)
                pe.wait_ge(s_g2, QT * (b + 1))
                for i in range(QT):
                    for k in range(XT):
                        mm = pe.matmul(ps[:, 4, i:i + 1], zs[:, k, i * P:(i + 1) * P], ones[:, 0:1],
                                       start=(k == 0), stop=(k == XT - 1))
                mm.then_inc(s_op, 1)
                for i in range(QT):
                    for k in range(XT):
                        mm = pe.matmul(ps[:, i, 0:D], yt[:, k, i * P:(i + 1) * P], wout_s[:, k, :],
                                       start=(k == 0), stop=(k == XT - 1))
                    mm.then_inc(s_op, 1)
                pe.wait_ge(s_blk, QT * (b + 1))
                for i in range(QT):
                    pe.wait_ge(s_xs1, b * QT + i + 1)
                    for k in range(DT):
                        mm = pe.transpose(ps[:, 2 + k, i * P:(i + 1) * P], xs1[:, i, k * P:(k + 1) * P], ident[:, :])
                mm.then_inc(s_xst1, 1)
                pe.wait_ge(s_xn1, DT * (b + 1))
                for item in LASTQ:
                    project(b, item)
                pass1_alone(b, G0, b + 1)
                pe.wait_ge(s_projfree, (b + 1) * NPJ + len(FRONT))
                for g in range(G1):
                    group(b, G0 + g, (b, G0 + g + 1) if g + 1 < G1 else (b + 1, 0))
                pe.wait_ge(s_norm, LEAD + b * NG + NG)
                for i in range(QT):
                    for g in range(G1):
                        mm = pe.matmul(ps[:, i, 0:D], ctxn[:, g, i * P:(i + 1) * P], wo1_s[:, g, :],
                                       start=(g == 0), stop=(g == G1 - 1))
                    mm.then_inc(s_o, 1)

        @block.scalar
        def _(act):
            act.wait_ge(s_w, 16 * (NLOAD + GH))
            nc.scalar.activation(a_c, a_c, ACT.Exp).then_inc(s_aconst, 1)
            act.wait_ge(s_dconst, DCONST)

            def high_part(b, item):
                layer, kind, i = item
                bank = pj_bank[item]
                if kind == "q":
                    for slot in range(2):
                        act.wait_ge(s_qst[slot], LEAD + b * QPER + (QCUM[1] if layer else 0))
                    dst, src = qhl[:, i, 0, :], ps[:, bank, 0:T]
                    bias, scale = (bq_c[:, i:i + 1], 1.0) if layer == 0 else (0.0, keep1_c)
                else:
                    if layer == 0:
                        for slot in range(2):
                            act.wait_ge(s_kst[slot], LEAD + b * KPER + (KCUM[0] if i[0] else 0))
                    elif i[0] == 0:
                        for slot in range(2):
                            act.wait_ge(s_kst[slot], LEAD + b * KPER + KCUM[1])
                    else:
                        act.wait_ge(s_kst[0], LEAD + b * KPER + KCUM[2])
                    c, w = KCH[i[1]]
                    dst, src = khl[:, 0, c:c + w], ps[:, bank, 0:w]
                    bias, scale = (bk_c[:, i[0]:i[0] + 1], 1.0) if layer == 0 else (0.0, 1.0)
                act.wait_ge(s_proj, b * NPJ + pj_index[item] + 1)
                nc.scalar.activation(dst, src, ACT.Identity, bias=bias, scale=scale).then_inc(s_hi, 1)

            def exponentials(b, gi):
                scale = (HD0 if gi < G0 else HD1) ** -0.5
                for t in range(KT):
                    act.wait_ge(s_pv, LEAD + b * NG * KT + max(gi * KT + t - 1, 0))
                    for half in range(2):
                        act.wait_ge(s_s, b * 2 * NG * KT + (gi * KT + t) * 2 + half + 1)
                        nc.scalar.activation(PR[:, t % 2, 2 * half:2 * half + 2, :], ps[:, 2 * half:2 * half + 2, :],
                                             ACT.Exp, scale=scale).then_inc(s_p, 1)
                    if gi == 0:
                        for item in steps[t][1:]:
                            high_part(b, item)
                act.wait_ge(s_pv, LEAD + b * NG * KT + (gi + 1) * KT)
                g = gi if gi < G0 else gi - G0
                nc.scalar.activation(ctxn[:, g, :], ps[:, 6, :], ACT.Copy).then_inc(s_ctxn, 1)
                if gi >= G0:
                    act.wait_ge(s_norm, LEAD + b * NG + gi)
                    nc.scalar.activation(rs[:, :], ps[:, 7, :], ACT.Copy).then_inc(s_scopy, 1)

            act.nop(nofuse=True).then_inc(s_ctxn, LEAD)
            for item in FRONT:
                high_part(0, item)
            with act.Fori(0, B) as b:
                for gi in range(G0):
                    exponentials(b, gi)
                for item in SECOND[:NC]:
                    high_part(b, item)
                act.wait_ge(s_xst, b + 1)
                for k in range(DT):
                    nc.scalar.activation(xn[:, k, :], ps[:, k, :], ACT.Copy, scale=nw_c[:, k:k + 1]).then_inc(s_xn, 1)

                def copy_raw(n):
                    bank = (3 + n) % 4
                    act.wait_ge(s_in, b * (1 + NCH + XT) + 2 + n)
                    if n < 2:
                        act.wait_ge(s_pad, b + 1)
                    else:
                        act.wait_ge(s_conv4, b * NCH + n - 1)
                    nc.scalar.activation(rawc[:, n % 2, TAPS - 1:TAPS - 1 + T], ps[:, bank, :], ACT.Copy)\
                        .then_inc(s_rawcp, 1)

                copy_raw(0)
                copy_raw(1)
                act.wait_ge(s_sp, b * SPN + 2)
                nc.scalar.activation(sp_t[:, 2, :], sp_t[:, 1, :], ACT.Exp).then_inc(s_spe, 1)
                for n in range(NCH):
                    act.wait_ge(s_conv4, b * NCH + n + 1)
                    if n >= 2:
                        act.wait_ge(s_xc, b * NCH + n - 1)
                    nc.scalar.activation(th[:, n % 2, :], xc[:, CORDER[n], :], ACT.Tanh).then_inc(s_th, 1)
                    if n + 2 < NCH:
                        copy_raw(n + 2)
                for n in range(XT):
                    act.wait_ge(s_in, b * (1 + NCH + XT) + 2 + NCH + n)
                    if n < 2:
                        act.wait_ge(s_xc, b * NCH + NCH - 1 + n)
                    else:
                        act.wait_ge(s_zs, b * XT + n - 1)
                    nc.scalar.activation(th[:, n % 2, :], ps[:, (3 + NCH + n) % 4, :], ACT.Tanh, scale=0.5)\
                        .then_inc(s_zth, 1)
                act.wait_ge(s_dps, b + 1)
                nc.scalar.activation(dec[:, :, :].rearrange("p a n -> p (a n)"), ps[:, 4, 0:2 * QT * HM], ACT.Exp)\
                    .then_inc(s_dec, 1)

                def square(c):
                    act.wait_ge(s_g, b * QT + c + 1)
                    cs = slice(c * P, (c + 1) * P)
                    nc.scalar.activation(zs[:, :, cs], yt[:, :, cs], ACT.Square).then_inc(s_g2, 1)

                for c in range(QT):
                    nb = b * QT + c
                    act.wait_ge(s_D, nb + 1)
                    act.wait_ge(s_yp, LEAD + nb)
                    nc.scalar.activation(Ld[:, :, :].rearrange("p h t -> p (h t)"),
                                         ps[:, 4:6, :].rearrange("p a n -> p (a n)"), ACT.Exp).then_inc(s_Ld, 1)
                    if c < QT - 1:
                        act.wait_ge(s_bt, b * (QT - 1) + c + 1)
                        if c > 0:
                            act.wait_ge(s_hp, b * (QT - 1) + c)
                        nc.scalar.activation(btok[:, :], ps[:, 3, 0:P], ACT.Copy).then_inc(s_btok, 1)
                    if c > 0:
                        act.wait_ge(s_cum, b * (QT - 1) + c)
                        nc.scalar.activation(Ce[:, :, :].rearrange("p h t -> p (h t)"),
                                             ps[:, 4:6, :].rearrange("p a n -> p (a n)"), ACT.Exp)\
                            .then_inc(s_Ecb, 1)
                        square(c - 1)
                square(QT - 1)
                for item in SECOND[NC + KT:]:
                    high_part(b, item)
                act.wait_ge(s_xst1, b + 1)
                for k in range(DT):
                    nc.scalar.activation(xn[:, k, :], ps[:, 2 + k, :], ACT.Identity, bias=cab_c[:, k:k + 1],
                                         scale=caw_c[:, k:k + 1]).then_inc(s_xn1, 1)
                for item in LASTQ:
                    high_part(b, item)
                for item in FRONT:
                    high_part(b + 1, item)
                for g in range(G1):
                    exponentials(b, G0 + g)

        @block.vector
        def _(dve):
            nconst = [0]

            def const(ins):
                ins.then_inc(s_dconst, 1)
                nconst[0] += 1

            for i in range(2):
                const(nc.vector.memset(f(KS[i][0:96, :, :]), 0.0))
                const(nc.vector.memset(f(KS[i][96:128, :, :]), 1.0))
                const(nc.vector.memset(f(QS[i][:, :, :]), 0.0))
            const(nc.vector.memset(vbuf[:, :], 0.0))
            dve.wait_ge(s_w, 16 * (NLOAD + GH))
            dve.wait_ge(s_const, 9)
            const(nc.vector.tensor_copy(identb[:, :], ident[:, :]))
            const(nc.vector.tensor_scalar(cw_c, cw_c, 0.5, None, ALU.mult))
            const(nc.vector.tensor_scalar(cb_c, cb_c, 0.5, None, ALU.mult))
            dve.wait_ge(s_aconst, 1)
            const(nc.vector.tensor_scalar(a_c, a_c, -1.0, None, ALU.mult))
            for k in range(XT):
                const(nc.vector.tensor_scalar(wout_s[:, k, :], wout_s[:, k, :], gw_c[:, k:k + 1], None, ALU.mult))
            const(nc.vector.tensor_reduce(small[:, 0:1], mask1_s, AX.X, ALU.min))
            const(nc.vector.tensor_scalar(m1row[:, 0:S], mask1_s[0:1, :], MASKED, None, ALU.mult))
            const(nc.vector.memset(m1row[:, S:SP], PADDED))
            dve.wait_ge(s_dconst, nconst[0])
            const(nc.vector.tensor_scalar(keep1_c, small[:, 0:1], -1.0, 1.0, ALU.mult, ALU.add))
            const(nc.vector.memset(zero_rows, 0.0))
            const(nc.vector.memset(one_row, 1.0))
            const(nc.vector.memset(small[:, 1:2], 0.0))
            assert nconst[0] == DCONST, nconst[0]
            dve.wait_ge(s_dconst, DCONST)

            def take(b, item):
                layer, kind, i = item
                n, bank = pj_index[item], pj_bank[item]
                if kind == "v":
                    dve.wait_ge(s_proj, b * NPJ + n + 1)
                    rows = P if i < KT - 1 else LAST
                    if layer == 0:
                        nc.vector.tensor_tensor(
                            v0[0:rows, i, 0:H0 * VW].rearrange("p (h c) -> p h c", c=VW)[:, :, 0:HD0],
                            ps[0:rows, bank, 0:D].rearrange("p (h c) -> p h c", c=HD0),
                            bv_s[0:rows, :].rearrange("p (h c) -> p h c", c=HD0), ALU.add).then_inc(s_projfree, 1)
                    else:
                        nc.vector.tensor_copy(v1[0:rows, i, :], ps[0:rows, bank, 0:D]).then_inc(s_projfree, 1)
                    return
                dve.wait_ge(s_hi, b * NHI + hi_index[item] + 1)
                if kind == "q":
                    hi, lo, src = qhl[:, i, 0, :], qhl[:, i, 1, :], ps[:, bank, 0:T]
                    scalar, op = (bq_c[:, i:i + 1], ALU.add) if layer == 0 else (keep1_c, ALU.mult)
                else:
                    c, w = KCH[i[1]]
                    hi, lo, src = khl[:, 0, c:c + w], khl[:, 1, c:c + w], ps[:, bank, 0:w]
                    scalar, op = (bk_c[:, i[0]:i[0] + 1], ALU.add) if layer == 0 else (1.0, ALU.mult)
                nc.vector.scalar_tensor_tensor(out=lo, in0=src, scalar=scalar, in1=f(hi), op0=op,
                                               op1=ALU.subtract).then_inc(s_projfree, 1)

            def raw_max(b, gi, k):
                idx = gi * RAW + k
                h, i, c = k // (QT * NC), k // NC % QT, k % NC
                c0, w = CHUNKS[c]
                dve.wait_ge(s_raw, b * NG * RAW + idx + 1)
                src, dst = ps[:, 4 + idx % 2, 0:w], mx[:, c, h * QT + i:h * QT + i + 1]
                if gi < G0:
                    alone(dve)
                    nc.vector.tensor_tensor_reduce(src, src, maskq[:, i, c0:c0 + w], 1.0, -3.0e38,
                                                   ALU.add, ALU.max, dst).then_inc(s_rawfree, 1)
                else:
                    nc.vector.tensor_reduce(dst, src, AX.X, ALU.max).then_inc(s_rawfree, 1)

            def maxima(b, gi):
                n = b * NG + gi + 1
                dve.wait_ge(s_rawfree, LEAD + b * NG * RAW + gi * RAW + RAW - 1)
                nc.vector.tensor_reduce(mxr[:, :], mx[:, :, :].rearrange("p c n -> p n c"), AX.X, ALU.max)\
                    .then_inc(s_mx, 1)
                dve.wait_ge(s_mx, n)
                nc.vector.tensor_scalar(nm[:, 0:16], mxr[:, :], -1.0, None, ALU.mult).then_inc(s_mhi, 1)
                dve.wait_ge(s_mhi, n)
                nc.vector.scalar_tensor_tensor(out=nm[:, 16:32], in0=mxr[:, :], scalar=-1.0, in1=f(nm[:, 0:16]),
                                               op0=ALU.mult, op1=ALU.subtract).then_inc(s_nm, 1)

            def maxima_rows(b, gi):
                idx = gi * RAW + RAW - 1
                dve.wait_ge(s_raw, b * NG * RAW + idx + 1)
                if gi >= 2:
                    dve.wait_ge(s_mload[gi % 2], LEAD + b * MPER + 32 * (gi // 2))
                else:
                    dve.wait_ge(s_mload[gi % 2], LEAD + b * MPER)
                nc.vector.tensor_copy(mrow[gi % 2][:, :], ps[0:32, 4 + idx % 2, 0:P]).then_inc(s_mrow, 1)
                dve.wait_ge(s_mrow, b * NG + gi + 1)
                nc.vector.memset(small[:, 1:2], 0.0).then_inc(s_rawfree, 1)

            def divide(b, gi):
                n = b * NG + gi + 1
                if gi < G0:
                    dve.wait_ge(s_sum, b * G0 + gi + 1)
                else:
                    dve.wait_ge(s_scopy, b * G1 + gi - G0 + 1)
                    dve.wait_ge(s_ctxn, LEAD + n)
                dve.wait_ge(s_norm, LEAD + n - 1)
                nc.vector.reciprocal(rs[:, :], ps[:, 7, :] if gi < G0 else rs[:, :]).then_inc(s_rs, 1)
                dve.wait_ge(s_rs, n)
                g = gi if gi < G0 else gi - G0
                nc.vector.tensor_tensor(ctxn[:, g, :], ctxn[:, g, :], rs[:, :], ALU.mult).then_inc(s_norm, 1)

            def group(b, gi, follow):
                for t in range(KT + 1):
                    if t == 0 and gi > G0:
                        divide(b, gi - 1)
                    if t == 0 and 0 < gi < G0:
                        divide(b, gi - 1)
                    if follow and follow[1] == 0 and t == 1:
                        dve.wait_ge(s_conv, follow[0] * NPIECE + QT * NC)
                    for slot in range(SLOTS):
                        if gi == 0 and slot == GH and t < KT:
                            take(b, steps[t][0])
                        if follow:
                            for k in raw_after(t, slot):
                                raw_max(*follow, k)
                    if gi == 0 and t < KT:
                        for item in steps[t][1:]:
                            take(b, item)
                    if follow and t == KT - 3:
                        maxima(*follow)
                    if follow and t == KT - 2:
                        maxima_rows(*follow)

            for first in (s_rawfree, s_norm, s_h, s_fin):
                dve.nop(nofuse=True).then_inc(first, LEAD)
            def pass1_alone(b, gi, bf):
                front = list(FRONT)
                for k in range(RAW - 1):
                    raw_max(b, gi, k)
                    if bf is not None and k % FEVERY == FEVERY - 1 and front:
                        take(bf, front.pop(0))
                maxima(b, gi)
                maxima_rows(b, gi)

            for item in FRONT:
                take(0, item)
            dve.wait_ge(s_conv, QT * NC)
            pass1_alone(0, 0, None)
            with dve.Fori(0, B) as b:
                for g in range(G0):
                    group(b, g, (b, g + 1) if g + 1 < G0 else None)
                divide(b, G0 - 1)
                second = list(SECOND[:NC + KT])
                late = list(SECOND[NC + KT:])

                def fill(n, items):
                    for _ in range(min(n, len(items))):
                        take(b, items.pop(0))

                dve.wait_ge(s_xb, QT * (b + 1))
                for i in range(QT):
                    n = b * QT + i + 1
                    dve.wait_ge(s_o, b * 2 * QT + i + 1)
                    nc.vector.tensor_tensor(xres[:, i, :], ps[:, i, 0:D], xres[:, i, :], ALU.add).then_inc(s_y, 1)
                    dve.wait_ge(s_y, n)
                    nc.vector.bn_stats(stats[:, i, :], xres[:, i, :]).then_inc(s_st, 1)
                    dve.wait_ge(s_st, n)
                    alone(dve)
                    nc.vector.bn_aggr(moments[:, i, :], stats[:, i, :]).then_inc(s_mom, 1)
                fill(4, second)
                dve.wait_ge(s_rstd, b + 1)
                dve.wait_ge(s_mom, QT * (b + 1))
                for i in range(QT):
                    n = b * QT + i + 1
                    nc.vector.tensor_scalar(xres[:, i, :], xres[:, i, :], moments[:, i, 0:1], rstd[:, 0, i:i + 1],
                                            ALU.subtract, ALU.mult).then_inc(s_ln[0], 1)
                    dve.wait_ge(s_ln[0], n)
                    nc.vector.tensor_tensor(xres[:, i, :], xres[:, i, :], lng_s[:, :], ALU.mult).then_inc(s_ln[1], 1)
                    dve.wait_ge(s_ln[1], n)
                    nc.vector.tensor_tensor(xres[:, i, :], xres[:, i, :], lnb_s[:, :], ALU.add).then_inc(s_ln[2], 1)
                    dve.wait_ge(s_ln[2], n)
                    nc.vector.tensor_tensor_reduce(xs[:, i, :], xres[:, i, :], xres[:, i, :], 1.0, 0.0, ALU.mult,
                                                   ALU.add, stats[:, i, 0:1]).then_inc(s_sq, 1)
                fill(4, second)
                dve.wait_ge(s_rms, b + 1)
                dve.wait_ge(s_sq, QT * (b + 1))
                for i in range(QT):
                    nc.vector.tensor_scalar(xs[:, i, :], xres[:, i, :], rstd[:, 1, i:i + 1], None, ALU.mult)\
                        .then_inc(s_xs, 1)
                fill(1, second)
                done = [0]

                def step(ins):
                    done[0] += 1
                    ins.then_inc(s_sp, 1)
                    dve.wait_ge(s_sp, b * SPN + done[0])

                X, NAB, U, R, Z, Z2, ACC, W = range(8)
                sl = lambda i: sp_t[:, i, :]
                dve.wait_ge(s_in, b * (1 + NCH + XT) + 1)
                step(nc.vector.tensor_tensor(sl(X).rearrange("p (c h) -> p c h", h=HM),
                                             ps[:, 2, 0:QT * HM].rearrange("p (c h) -> p c h", h=HM),
                                             dtb_c.unsqueeze(1).broadcast_to([P, QT, HM]), ALU.add))
                nc.vector.scalar_tensor_tensor(out=sl(NAB), in0=sl(X), scalar=-1.0, in1=sl(X), op0=ALU.mult,
                                               op1=ALU.min).then_inc(s_sp, 1)
                done[0] += 1
                dve.wait_ge(s_spe, b + 1)
                step(nc.vector.tensor_scalar(sl(R), sl(U), 2.0, None, ALU.add))
                step(nc.vector.reciprocal(sl(W), sl(R)))
                step(nc.vector.tensor_tensor(sl(Z), sl(U), sl(W), ALU.mult))
                step(nc.vector.tensor_tensor(sl(Z2), sl(Z), sl(Z), ALU.mult))
                step(nc.vector.tensor_scalar(sl(ACC), sl(Z2), ATANH[0], None, ALU.mult))
                for co in ATANH[1:]:
                    step(nc.vector.scalar_tensor_tensor(out=sl(ACC), in0=sl(ACC), scalar=co, in1=sl(Z2),
                                                        op0=ALU.add, op1=ALU.mult))
                step(nc.vector.scalar_tensor_tensor(out=sl(ACC), in0=sl(ACC), scalar=1.0, in1=sl(Z), op0=ALU.add,
                                                    op1=ALU.mult))
                step(nc.vector.tensor_scalar(sl(R), sl(X), 0.0, None, ALU.max))
                step(nc.vector.scalar_tensor_tensor(out=dtt[:, :, :].rearrange("p c h -> p (c h)"), in0=sl(ACC),
                                                    scalar=2.0, in1=sl(R), op0=ALU.mult, op1=ALU.add))
                assert done[0] == SPN, done[0]
                nc.vector.tensor_tensor(aa[:, :, :], dtt[:, :, :], a_c.unsqueeze(1).broadcast_to([P, QT, HM]),
                                        ALU.mult).then_inc(s_a, 1)

                def convolve(n):
                    ch = CORDER[n]
                    dve.wait_ge(s_rawcp, b * NCH + n + 1)
                    r = rawc[:, n % 2, :]
                    o = xc[:, ch, :]
                    w = cw_c[:, ch * TAPS:(ch + 1) * TAPS]
                    nc.vector.tensor_scalar(o, r[:, 0:T], w[:, 0:1], cb_c[:, ch:ch + 1], ALU.mult, ALU.add)\
                        .then_inc(s_cv, 1)
                    for k in range(1, TAPS):
                        dve.wait_ge(s_cv, (b * NCH + n) * (TAPS - 1) + k)
                        ins = nc.vector.scalar_tensor_tensor(out=o, in0=r[:, k:k + T], scalar=w[:, k:k + 1], in1=o,
                                                             op0=ALU.mult, op1=ALU.add)
                        ins.then_inc(s_cv if k < TAPS - 1 else s_conv4, 1)

                def gate_conv(n):
                    dve.wait_ge(s_th, b * NCH + n + 1)
                    nc.vector.scalar_tensor_tensor(out=xc[:, CORDER[n], :], in0=th[:, n % 2, :], scalar=1.0,
                                                   in1=xc[:, CORDER[n], :], op0=ALU.add, op1=ALU.mult)\
                        .then_inc(s_xc, 1)

                for n in range(NCH + 1):
                    if n < NCH:
                        convolve(n)
                    if n >= 1:
                        gate_conv(n - 1)
                for n in range(XT):
                    dve.wait_ge(s_zth, b * XT + n + 1)
                    nc.vector.scalar_tensor_tensor(out=zs[:, n, :], in0=th[:, n % 2, :], scalar=1.0,
                                                   in1=ps[:, (3 + NCH + n) % 4, :], op0=ALU.add, op1=ALU.mult)\
                        .then_inc(s_zs, 1)
                dve.wait_ge(s_xc, NCH * (b + 1))
                dve.wait_ge(s_zs, XT * (b + 1))
                for c in range(QT):
                    nb = b * QT + c
                    cs = slice(c * P, (c + 1) * P)
                    dve.wait_ge(s_G, nb + 1)
                    nc.vector.tensor_tensor(GM[:, :], ps[:, 1, 0:P], upto[:, :], ALU.mult).then_inc(s_GM, 1)
                    dve.wait_ge(s_tok, nb + 1)
                    dve.wait_ge(s_yp, LEAD + nb)
                    if c > 0:
                        dve.wait_ge(s_dx2, b * (QT - 1) + c)
                    nc.vector.tensor_tensor(dx[:, :].rearrange("p (h e) -> p h e", h=HM),
                                            ps[:, 0, :].rearrange("p (h e) -> p h e", h=HM),
                                            dtt[:, c, :].unsqueeze(2).broadcast_to([P, HM, PD]), ALU.mult)\
                        .then_inc(s_dx, 1)
                    dve.wait_ge(s_Ld, nb + 1)
                    dve.wait_ge(s_GM, nb + 1)
                    nc.vector.tensor_tensor(Ld[:, :, :], Ld[:, :, :], GM[:, :].unsqueeze(1).broadcast_to([P, HM, P]),
                                            ALU.mult).then_inc(s_M, 1)
                    fill(1, second)
                    dve.wait_ge(s_yp, LEAD + nb + 1)
                    for i in range(XT):
                        nc.vector.scalar_tensor_tensor(out=yt[:, i, cs], in0=xc[:, i, cs], scalar=dsk_c[:, i:i + 1],
                                                       in1=ps[:, 2, i * P:(i + 1) * P], op0=ALU.mult, op1=ALU.add)\
                            .then_inc(s_yt, 1)
                    if c < QT - 1:
                        dve.wait_ge(s_hp, b * (QT - 1) + c + 1)
                        if c == 0:
                            nc.vector.tensor_copy(Hst[:, :], ps[:, 3, :]).then_inc(s_h, 1)
                        else:
                            dve.wait_ge(s_hs, b * (QT - 2) + c)
                            nc.vector.tensor_tensor(Hst[:, :], ps[:, 3, :], Hst[:, :], ALU.add).then_inc(s_h, 1)
                    dve.wait_ge(s_yt, (nb + 1) * XT)
                    nc.vector.tensor_tensor(yt[:, :, cs], yt[:, :, cs], zs[:, :, cs], ALU.mult).then_inc(s_g, 1)
                fill(len(second), second)
                fill(len(late), late)
                dve.wait_ge(s_op, b * (1 + QT) + 1)
                nc.vector.tensor_copy(stats[:, :, 0], ps[:, 4, 0:QT]).then_inc(s_ssq, 1)
                dve.wait_ge(s_gr, b + 1)
                for i in range(QT):
                    n = b * QT + i + 1
                    dve.wait_ge(s_op, b * (1 + QT) + 2 + i)
                    nc.vector.scalar_tensor_tensor(out=xres[:, i, :], in0=ps[:, i, 0:D], scalar=rstd[:, 2, i:i + 1],
                                                   in1=xres[:, i, :], op0=ALU.mult, op1=ALU.add).then_inc(s_blk, 1)
                    dve.wait_ge(s_blk, n)
                    nc.vector.bn_stats(stats[:, i, :], xres[:, i, :]).then_inc(s_st1, 1)
                    dve.wait_ge(s_st1, n)
                    alone(dve)
                    nc.vector.bn_aggr(moments[:, i, :], stats[:, i, :]).then_inc(s_mom1, 1)
                dve.wait_ge(s_rstd1, b + 1)
                dve.wait_ge(s_mom1, QT * (b + 1))
                for i in range(QT):
                    nc.vector.tensor_scalar(xs1[:, i, :], xres[:, i, :], moments[:, i, 0:1], rstd[:, 0, i:i + 1],
                                            ALU.subtract, ALU.mult).then_inc(s_xs1, 1)
                for item in LASTQ:
                    take(b, item)
                pass1_alone(b, G0, b + 1)
                for g in range(G1):
                    group(b, G0 + g, (b, G0 + g + 1) if g + 1 < G1 else (b + 1, 0))
                divide(b, NG - 1)
                for i in range(QT):
                    dve.wait_ge(s_o, b * 2 * QT + QT + i + 1)
                    nc.vector.tensor_tensor(xres[:, i, :], ps[:, i, 0:D], xres[:, i, :], ALU.add).then_inc(s_fin, 1)


def _by_channel(a, head_width, np):
    n = a.shape[-1]
    a = a.reshape(a.shape[:-1] + (n // (GH * head_width), GH, head_width))
    return np.ascontiguousarray(np.swapaxes(a, -1, -2).reshape(a.shape[:-3] + (n,)))


def kernel(**inputs):
    import numpy as np
    import concourse.bacc as bacc
    from concourse.bass_utils import run_bass_kernel_spmd as run

    i = {k: np.asarray(v) for k, v in inputs.items()}
    c = np.ascontiguousarray
    tr = lambda a: c(np.swapaxes(a, -1, -2))
    x, context, mask = i["x"], i["ctx_1024"], i["mask_BxSxS2_ik1"]
    laid = {
        "x": c(x), "xt": tr(x), "ctxt": tr(context), "mask": c(mask), "maskt": tr(mask),
        "mask1": c(i["mask_1xS2_bf0"]),
        "wq0": _by_channel(tr(i["L0_xattn_Wq"]), HD0, np), "bq0": _by_channel(i["L0_xattn_bq"], HD0, np),
        "wk0": _by_channel(tr(i["L0_xattn_Wk"]), HD0, np), "bk0": _by_channel(i["L0_xattn_bk"], HD0, np),
        "wv0": tr(i["L0_xattn_Wv"]), "bv0": c(i["L0_xattn_bv"]),
        "wo0": tr(i["L0_xattn_Wo"]), "bo0": c(i["L0_xattn_bo"]),
        "ln_g": c(i["L0_xattn_ln_g"]), "ln_b": c(i["L0_xattn_ln_b"]),
        "norm_w": c(i["L1_xattn_m_norm_w"]), "w_in": c(i["L1_xattn_in_proj_w"]),
        "conv_w": c(i["L1_xattn_conv_w"]), "conv_b": c(i["L1_xattn_conv_b"]),
        "dt_bias": c(i["L1_xattn_dt_bias"]), "a_log": c(i["L1_xattn_A_log"]), "d_skip": c(i["L1_xattn_D_skip"]),
        "gnorm_w": c(i["L1_xattn_gnorm_w"]), "w_out": c(i["L1_xattn_out_proj_w"]),
        "ca_w": c(i["L1_xattn_ca_ln_w"]), "ca_b": c(i["L1_xattn_ca_ln_b"]),
        "wq1": _by_channel(i["L1_xattn_Wq"], HD1, np), "wk1": _by_channel(i["L1_xattn_Wk"], HD1, np),
        "wv1": c(i["L1_xattn_Wv"]), "wo1": c(i["L1_xattn_Wo"]),
    }
    nc = bacc.Bacc("TRN2", target_bir_lowering=False, num_devices=1, dynamic_dma_scratch_size=1024)
    arrays = {f"in_{k}": a for k, a in laid.items()}
    args = [nc.dram_tensor(f"in_{k}", a.shape, mybir.dt.from_np(a.dtype), kind="ExternalInput").ap()
            for k, a in laid.items()]
    out = nc.dram_tensor("out_0", x.shape, mybir.dt.from_np(x.dtype), kind="ExternalOutput").ap()
    xattn_mamba(nc, *args, out)
    return run(nc, [arrays], core_ids=[0]).results[0]["out_0"]
```
